# Optimizing a Trainium2 kernel written in Bass

```python
import numpy as np
import jax
import jax.numpy as jnp

def _softmax(x, axis=-1):
    return jax.nn.softmax(x, axis=axis)

def _gelu(x):
    return jax.nn.gelu(x, approximate=True)

def _silu(x):
    return jax.nn.silu(x)

def _sigmoid(x):
    return jax.nn.sigmoid(x)

def _layernorm(x, axis=-1, eps=1e-05):
    m = jnp.mean(x, axis=axis, keepdims=True)
    v = jnp.var(x, axis=axis, keepdims=True)
    return (x - m) / jnp.sqrt(v + eps)

def _scatter_add(tgt, idx, src, axis=0):
    return tgt.at[idx].add(src)

def _segment_sum(src, seg, n):
    return jax.ops.segment_sum(src, seg, n)
kernel_name = 'mk_dlrm_tower_d1_rec_r8_d90431'

def setup_inputs(seed: int=0):
    np.random.seed(seed)
    _w = jnp.asarray

    def _rec_inputs():
        import jax
        import jax.numpy as jnp
        _tk = jax.random.key(seed)
        dense_ctx = jax.random.normal(jax.random.fold_in(_tk, 190), (1024, 16), jnp.float32)
        ids = jnp.stack([jax.random.randint(jax.random.fold_in(_tk, 200 + f), (1024,), 0, v, jnp.int32) for f, v in enumerate([125000, 1000, 125000, 12500, 125000, 12500, 1250, 1000, 12500, 1000, 12500, 1000, 12500, 1250, 1250, 12500, 12500, 1000, 12500, 1250, 1250, 1000, 1250, 1250, 1250, 1250, 1000, 1000, 1000, 1000, 1000, 1000])], axis=1)
        tbl_0 = 0.05 * jax.random.normal(jax.random.fold_in(_tk, 500 + 0), (125000, 64), jnp.float32)
        tbl_1 = 0.05 * jax.random.normal(jax.random.fold_in(_tk, 500 + 1), (1000, 64), jnp.float32)
        tbl_2 = 0.05 * jax.random.normal(jax.random.fold_in(_tk, 500 + 2), (125000, 64), jnp.float32)
        tbl_3 = 0.05 * jax.random.normal(jax.random.fold_in(_tk, 500 + 3), (12500, 64), jnp.float32)
        tbl_4 = 0.05 * jax.random.normal(jax.random.fold_in(_tk, 500 + 4), (125000, 64), jnp.float32)
        tbl_5 = 0.05 * jax.random.normal(jax.random.fold_in(_tk, 500 + 5), (12500, 64), jnp.float32)
        tbl_6 = 0.05 * jax.random.normal(jax.random.fold_in(_tk, 500 + 6), (1250, 64), jnp.float32)
        tbl_7 = 0.05 * jax.random.normal(jax.random.fold_in(_tk, 500 + 7), (1000, 64), jnp.float32)
        tbl_8 = 0.05 * jax.random.normal(jax.random.fold_in(_tk, 500 + 8), (12500, 64), jnp.float32)
        tbl_9 = 0.05 * jax.random.normal(jax.random.fold_in(_tk, 500 + 9), (1000, 64), jnp.float32)
        tbl_10 = 0.05 * jax.random.normal(jax.random.fold_in(_tk, 500 + 10), (12500, 64), jnp.float32)
        tbl_11 = 0.05 * jax.random.normal(jax.random.fold_in(_tk, 500 + 11), (1000, 64), jnp.float32)
        tbl_12 = 0.05 * jax.random.normal(jax.random.fold_in(_tk, 500 + 12), (12500, 64), jnp.float32)
        tbl_13 = 0.05 * jax.random.normal(jax.random.fold_in(_tk, 500 + 13), (1250, 64), jnp.float32)
        tbl_14 = 0.05 * jax.random.normal(jax.random.fold_in(_tk, 500 + 14), (1250, 64), jnp.float32)
        tbl_15 = 0.05 * jax.random.normal(jax.random.fold_in(_tk, 500 + 15), (12500, 64), jnp.float32)
        tbl_16 = 0.05 * jax.random.normal(jax.random.fold_in(_tk, 500 + 16), (12500, 64), jnp.float32)
        tbl_17 = 0.05 * jax.random.normal(jax.random.fold_in(_tk, 500 + 17), (1000, 64), jnp.float32)
        tbl_18 = 0.05 * jax.random.normal(jax.random.fold_in(_tk, 500 + 18), (12500, 64), jnp.float32)
        tbl_19 = 0.05 * jax.random.normal(jax.random.fold_in(_tk, 500 + 19), (1250, 64), jnp.float32)
        tbl_20 = 0.05 * jax.random.normal(jax.random.fold_in(_tk, 500 + 20), (1250, 64), jnp.float32)
        tbl_21 = 0.05 * jax.random.normal(jax.random.fold_in(_tk, 500 + 21), (1000, 64), jnp.float32)
        tbl_22 = 0.05 * jax.random.normal(jax.random.fold_in(_tk, 500 + 22), (1250, 64), jnp.float32)
        tbl_23 = 0.05 * jax.random.normal(jax.random.fold_in(_tk, 500 + 23), (1250, 64), jnp.float32)
        tbl_24 = 0.05 * jax.random.normal(jax.random.fold_in(_tk, 500 + 24), (1250, 64), jnp.float32)
        tbl_25 = 0.05 * jax.random.normal(jax.random.fold_in(_tk, 500 + 25), (1250, 64), jnp.float32)
        tbl_26 = 0.05 * jax.random.normal(jax.random.fold_in(_tk, 500 + 26), (1000, 64), jnp.float32)
        tbl_27 = 0.05 * jax.random.normal(jax.random.fold_in(_tk, 500 + 27), (1000, 64), jnp.float32)
        tbl_28 = 0.05 * jax.random.normal(jax.random.fold_in(_tk, 500 + 28), (1000, 64), jnp.float32)
        tbl_29 = 0.05 * jax.random.normal(jax.random.fold_in(_tk, 500 + 29), (1000, 64), jnp.float32)
        tbl_30 = 0.05 * jax.random.normal(jax.random.fold_in(_tk, 500 + 30), (1000, 64), jnp.float32)
        tbl_31 = 0.05 * jax.random.normal(jax.random.fold_in(_tk, 500 + 31), (1000, 64), jnp.float32)
        _rk = jax.random.fold_in(_tk, 7)
        W_top1 = 0.0441942 * jax.random.normal(jax.random.fold_in(_tk, 801), (512, 512), jnp.float32)
        W_top2 = 0.0441942 * jax.random.normal(jax.random.fold_in(_tk, 802), (512, 256), jnp.float32)
        W_top3 = 0.0625 * jax.random.normal(jax.random.fold_in(_tk, 803), (256, 1), jnp.float32)
        b_top1 = jnp.zeros((512,), jnp.float32)
        b_top2 = jnp.zeros((256,), jnp.float32)
        return (dense_ctx, ids, tbl_0, tbl_1, tbl_2, tbl_3, tbl_4, tbl_5, tbl_6, tbl_7, tbl_8, tbl_9, tbl_10, tbl_11, tbl_12, tbl_13, tbl_14, tbl_15, tbl_16, tbl_17, tbl_18, tbl_19, tbl_20, tbl_21, tbl_22, tbl_23, tbl_24, tbl_25, tbl_26, tbl_27, tbl_28, tbl_29, tbl_30, tbl_31, W_top1, b_top1, W_top2, b_top2, W_top3)
    dense_ctx, ids, tbl_0, tbl_1, tbl_2, tbl_3, tbl_4, tbl_5, tbl_6, tbl_7, tbl_8, tbl_9, tbl_10, tbl_11, tbl_12, tbl_13, tbl_14, tbl_15, tbl_16, tbl_17, tbl_18, tbl_19, tbl_20, tbl_21, tbl_22, tbl_23, tbl_24, tbl_25, tbl_26, tbl_27, tbl_28, tbl_29, tbl_30, tbl_31, W_top1, b_top1, W_top2, b_top2, W_top3 = _rec_inputs()

    def _L0_rec_setup():
        import jax, jax.numpy as jnp
        import numpy as np
        key = jax.random.key(seed)
        k1, k2 = jax.random.split(key)
        B, F, D = (512, 32, 64)
        P = F * (F - 1) // 2
        x = jax.random.normal(k1, (B, F, D), dtype=jnp.float32)
        W = jax.random.normal(k2, (P, D, D), dtype=jnp.float32) * (1.0 / np.sqrt(D))
        return {'x': x, 'W': W}
    _L0_rec_all = _L0_rec_setup()
    _L0_rec_in = {k: v for k, v in _L0_rec_all.items() if k in ('W',)}
    del _L0_rec_all
    return {'dense_ctx': dense_ctx, 'ids': ids, 'tbl_0': tbl_0, 'tbl_1': tbl_1, 'tbl_2': tbl_2, 'tbl_3': tbl_3, 'tbl_4': tbl_4, 'tbl_5': tbl_5, 'tbl_6': tbl_6, 'tbl_7': tbl_7, 'tbl_8': tbl_8, 'tbl_9': tbl_9, 'tbl_10': tbl_10, 'tbl_11': tbl_11, 'tbl_12': tbl_12, 'tbl_13': tbl_13, 'tbl_14': tbl_14, 'tbl_15': tbl_15, 'tbl_16': tbl_16, 'tbl_17': tbl_17, 'tbl_18': tbl_18, 'tbl_19': tbl_19, 'tbl_20': tbl_20, 'tbl_21': tbl_21, 'tbl_22': tbl_22, 'tbl_23': tbl_23, 'tbl_24': tbl_24, 'tbl_25': tbl_25, 'tbl_26': tbl_26, 'tbl_27': tbl_27, 'tbl_28': tbl_28, 'tbl_29': tbl_29, 'tbl_30': tbl_30, 'tbl_31': tbl_31, 'W_top1': W_top1, 'b_top1': b_top1, 'W_top2': W_top2, 'b_top2': b_top2, 'W_top3': W_top3, 'L0_rec_W': _L0_rec_in['W']}

def reference(dense_ctx, ids, tbl_0, tbl_1, tbl_2, tbl_3, tbl_4, tbl_5, tbl_6, tbl_7, tbl_8, tbl_9, tbl_10, tbl_11, tbl_12, tbl_13, tbl_14, tbl_15, tbl_16, tbl_17, tbl_18, tbl_19, tbl_20, tbl_21, tbl_22, tbl_23, tbl_24, tbl_25, tbl_26, tbl_27, tbl_28, tbl_29, tbl_30, tbl_31, W_top1, b_top1, W_top2, b_top2, W_top3, L0_rec_W):
    import jax
    import jax.numpy as jnp

    def _L0_rec_ref(x, W):
        import jax, jax.numpy as jnp
        import numpy as np
        F = x.shape[1]
        idx_i, idx_j = np.triu_indices(F, k=1)
        xi = x[:, idx_i, :]
        xj = x[:, idx_j, :]
        left = jnp.einsum('bpd,pde->bpe', xi, W)
        out = jnp.sum(left * xj, axis=-1)
        return out
    e = jnp.stack([tbl_0[ids[:, 0]], tbl_1[ids[:, 1]], tbl_2[ids[:, 2]], tbl_3[ids[:, 3]], tbl_4[ids[:, 4]], tbl_5[ids[:, 5]], tbl_6[ids[:, 6]], tbl_7[ids[:, 7]], tbl_8[ids[:, 8]], tbl_9[ids[:, 9]], tbl_10[ids[:, 10]], tbl_11[ids[:, 11]], tbl_12[ids[:, 12]], tbl_13[ids[:, 13]], tbl_14[ids[:, 14]], tbl_15[ids[:, 15]], tbl_16[ids[:, 16]], tbl_17[ids[:, 17]], tbl_18[ids[:, 18]], tbl_19[ids[:, 19]], tbl_20[ids[:, 20]], tbl_21[ids[:, 21]], tbl_22[ids[:, 22]], tbl_23[ids[:, 23]], tbl_24[ids[:, 24]], tbl_25[ids[:, 25]], tbl_26[ids[:, 26]], tbl_27[ids[:, 27]], tbl_28[ids[:, 28]], tbl_29[ids[:, 29]], tbl_30[ids[:, 30]], tbl_31[ids[:, 31]]], axis=1)
    z = _L0_rec_ref(e, L0_rec_W)
    z = z.reshape(z.shape[0], -1)
    h = jnp.concatenate([z, dense_ctx], axis=1)
    h = jnp.maximum(h @ W_top1 + b_top1, 0.0)
    h = jnp.maximum(h @ W_top2 + b_top2, 0.0)
    y = h @ W_top3
    return y

_drawn_inputs = setup_inputs


def setup_inputs(seed=0):
    import zlib

    import numpy as np

    out = dict(_drawn_inputs(seed))
    spreads = {'b_top1': (0.0, 0.1), 'b_top2': (0.0, 0.1)}
    factors = {}
    for name, (base, spread) in spreads.items():
        noise = np.random.default_rng([zlib.crc32(name.encode()), seed]).standard_normal(out[name].shape)
        drawn = base * np.exp(spread * noise) if base else spread * noise
        out[name] = jnp.asarray(drawn.astype(out[name].dtype))
    for name, factor in factors.items():
        out[name] = (out[name] * factor).astype(out[name].dtype)
    return out
```

```python
import concourse.bass as bass
from concourse import mybir
from contextlib import ExitStack

FP32 = mybir.dt.float32
INT32 = mybir.dt.int32
ALU = mybir.AluOpType
ACT = mybir.ActivationFunctionType

BATCH, FIELDS, DIM, DENSE = 1024, 32, 64, 16
PAIRS = FIELDS * (FIELDS - 1) // 2
HID1, HID2 = 512, 256
PART = 128
HALF = 512
HALVES = BATCH // HALF
TILES = HALF // PART
LEVELS = FIELDS // 2
KT = 4

STEPS = [(m, mp) for m in reversed(range(LEVELS)) for mp in range(m, LEVELS)]
NS = len(STEPS)
COL = {step: PART * n for n, step in enumerate(STEPS)}

BLOCKS = []
for n, (m, mp) in enumerate(STEPS):
    BLOCKS += [(n, 0)] if mp == m else [(n, 0), (n, 1)]
GROUP = 4
GROUPS = len(BLOCKS) // GROUP
GROUPS_PER_KT = GROUPS // KT
LAG = 2
LRING, PRING, XRING = 3, 5, 4

LAST_BLOCK_OF_STEP = {s: b for b, (s, _) in enumerate(BLOCKS)}


def pair_row(i, j):
    return i * (2 * FIELDS - i - 1) // 2 + j - i - 1


def groups_after(s):
    done = s - LAG
    return [g for g in range(GROUPS) if BLOCKS[GROUP * g + GROUP - 1][0] == done]


def groups_left():
    return [g for g in range(GROUPS) if BLOCKS[GROUP * g + GROUP - 1][0] > NS - 1 - LAG]


def transposes_after(m, mp):
    return mp == max(m, LEVELS - 2)


def place(block):
    g = block // GROUP
    return g // GROUPS_PER_KT, 32 * (block % GROUP) + 2 * (g % GROUPS_PER_KT)


def top1_runs():
    runs = {}
    singles = []
    for b, (s, side) in enumerate(BLOCKS):
        m, mp = STEPS[s]
        kt, part = place(b)
        if m == mp:
            singles.append((kt, part + 1, pair_row(2 * m, 2 * m + 1), 0))
            continue
        runs.setdefault((2 * m + side, kt, b % GROUP), []).append((part, pair_row(2 * m + side, 2 * mp)))
    out = []
    for (_, kt, _), rows in runs.items():
        at = 0
        for n in range(1, len(rows) + 1):
            if n == len(rows) or rows[n][0] != rows[n - 1][0] + 2 or rows[n][1] != rows[n - 1][1] + 4:
                out.append((kt, *rows[at], n - at))
                at = n
    return out + singles


def build(nc, dense_ctx, ids, tables, W_top1, b_top1, W_top2, b_top2, W_top3, W, y):
    ctx = ExitStack()
    with ctx:
        def sb(name, shape, dt=FP32):
            return ctx.enter_context(nc.sbuf_tensor(name, shape, dt))

        def sem(name):
            return ctx.enter_context(nc.semaphore(name))

        ids_sb = sb("ids_sb", [PART, BATCH // PART, FIELDS], INT32)
        dense_sb = sb("dense_sb", [PART, BATCH // PART, DENSE])
        rows = sb("rows", [PART, XRING, TILES, 2 * DIM])
        xT = sb("xT", [PART, HALVES, LEVELS, HALF])
        Wsb = sb("Wsb", [PART, NS * PART])
        prod = sb("prod", [PART, PRING, 2, HALF])
        w1 = sb("w1", [PART, KT, HID1])
        w1d = sb("w1d", [DENSE, HID1])
        w2 = sb("w2", [PART, HID1 // PART, HID2])
        w3 = sb("w3", [PART, HID2 // PART])
        b1 = sb("b1", [PART, HID1 // PART])
        b2 = sb("b2", [PART, HID2 // PART])
        zT = sb("zT", [PART, KT, HALF])
        denseT = sb("denseT", [DENSE, HALVES, HALF])
        h1T = sb("h1T", [PART, HID1 // PART, HALF])
        h2T = sb("h2T", [PART, HID2 // PART, HALF])
        ysb = sb("ysb", [1, HALVES, HALF])
        ident = sb("ident", [PART, PART])
        pick = sb("pick", [PART, 62])

        left = ctx.enter_context(nc.psum_tensor("left", [PART, LRING, 2, HALF], FP32))
        zacc = ctx.enter_context(nc.psum_tensor("zacc", [PART, HALF], FP32))
        xps = ctx.enter_context(nc.psum_tensor("xps", [PART, HALF], FP32))

        ids_in = sem("ids_in")
        dense_in = sem("dense_in")
        consts_in = sem("consts_in")
        w1_in = sem("w1_in")
        w1_zeroed = sem("w1_zeroed")
        w_zeroed = sem("w_zeroed")
        w_in = [sem(f"w_in{m}") for m in range(LEVELS)]
        rows_in = [sem(f"rows_in{r}") for r in range(XRING)]
        ident_zeroed = sem("ident_zeroed")
        ident_made = sem("ident_made")
        pick_zeroed = sem("pick_zeroed")
        pick_made = sem("pick_made")
        x_transposed = sem("x_transposed")
        x_ready = sem("x_ready")
        dense_transposed = sem("dense_transposed")
        dense_ready = sem("dense_ready")
        left_ready = sem("left_ready")
        prod_ready = sem("prod_ready")
        groups_summed = sem("groups_summed")
        z_ready = sem("z_ready")
        h1_summed = sem("h1_summed")
        h1_ready = sem("h1_ready")
        h2_summed = sem("h2_summed")
        h2_ready = sem("h2_ready")
        y_summed = sem("y_summed")
        y_ready = sem("y_ready")
        y_out = sem("y_out")

        runs = top1_runs()
        block = ctx.enter_context(nc.Block())

        @block.sync
        def _(sp):
            sp.dma_start(ids_sb[:, :, :], ids.rearrange("(t p) f -> p t f", p=PART)).then_inc(ids_in, 16)
            sp.dma_start(dense_sb[:, :, :], dense_ctx.rearrange("(t p) k -> p t k", p=PART)).then_inc(dense_in, 16)
            for m in reversed(range(LEVELS)):
                col = COL[(m, m)]
                for side in range(2):
                    i = 2 * m + side
                    n = FIELDS - 1 - i
                    if n == 0:
                        continue
                    at = col + (DIM if side == 0 else PART)
                    sp.dma_start(
                        Wsb[DIM * side:DIM * side + DIM, at:at + n * DIM].rearrange("d (p e) -> d p e", e=DIM),
                        W[pair_row(i, i + 1):pair_row(i, i + 1) + n, :, :].rearrange("p d e -> d p e"),
                    ).then_inc(w_in[m], 16)
            sp.wait_ge(w1_zeroed, 1)
            for kt, part, row, n in runs:
                if n == 0:
                    dst, src = w1[part:part + 1, kt, :], W_top1[row:row + 1, :]
                    sp.dma_start(dst, src).then_inc(w1_in, 16)
                else:
                    for two in range(2):
                        src = W_top1[row + two:row + two + 4 * (n - 1) + 1:4, :]
                        dst = w1[part + two:part + two + 2 * (n - 1) + 1:2, kt, :]
                        sp.dma_start(dst, src).then_inc(w1_in, 16)
            sp.dma_start(w1d[:, :], W_top1[PAIRS:PAIRS + DENSE, :]).then_inc(consts_in, 16)
            sp.dma_start(w2[:, :, :], W_top2.rearrange("(k p) n -> p k n", p=PART)).then_inc(consts_in, 16)
            sp.dma_start(w3[:, :], W_top3.rearrange("(k p) n -> p (k n)", p=PART),
                         allow_slow_non_contiguous=True).then_inc(consts_in, 16)
            sp.dma_start(b1[:, :], b_top1.rearrange("(k p) -> p k", p=PART),
                         allow_slow_non_contiguous=True).then_inc(consts_in, 16)
            sp.dma_start(b2[:, :], b_top2.rearrange("(k p) -> p k", p=PART),
                         allow_slow_non_contiguous=True).then_inc(consts_in, 16)
            for h in range(HALVES):
                sp.wait_ge(y_ready, h + 1)
                sp.dma_start(y[HALF * h:HALF * h + HALF, :].rearrange("b n -> n b"), ysb[0:1, h, :]).then_inc(y_out, 16)
            sp.wait_ge(y_out, 16 * HALVES)

        @block.gpsimd
        def _(pool):
            nc.gpsimd.memset(ident[:, :], 0.0).then_inc(ident_zeroed, 1)
            pool.wait_ge(ident_zeroed, 1)
            nc.gpsimd.affine_select(out=ident[:, :], in_=ident[:, :], compare_op=ALU.not_equal, fill=1.0,
                                    base=0, pattern=[[-1, PART]], channel_multiplier=1).then_inc(ident_made, 1)
            pool.wait_ge(ids_in, 16)
            for h in range(HALVES):
                for m in reversed(range(LEVELS)):
                    n = LEVELS * h + LEVELS - 1 - m
                    if n >= XRING:
                        pool.wait_ge(x_transposed, n - XRING + 1)
                    for t in range(TILES):
                        for side in range(2):
                            f = 2 * m + side
                            nc.gpsimd.indirect_dma_start(
                                rows[:, n % XRING, t, DIM * side:DIM * side + DIM], None, tables[f][:, :],
                                bass.IndirectOffsetOnAxis(ap=ids_sb[:, TILES * h + t, f:f + 1], axis=0),
                            ).then_inc(rows_in[n % XRING], 16)

        @block.tensor
        def _(pe):
            def transpose_level(n):
                pe.wait_ge(rows_in[n % XRING], 16 * 2 * TILES * (n // XRING + 1))
                if n == 0:
                    pe.wait_ge(ident_made, 1)
                    pe.wait_ge(dense_ready, HALVES)
                else:
                    pe.wait_ge(x_ready, n)
                for t in range(TILES):
                    last = nc.tensor.transpose(xps[:, PART * t:PART * t + PART], rows[:, n % XRING, t, :], ident[:, :])
                last.then_inc(x_transposed, 1)

            def sum_group(h, g):
                part, k = g // GROUPS_PER_KT, g % GROUPS_PER_KT
                pe.wait_ge(prod_ready, NS * h + BLOCKS[GROUP * g + GROUP - 1][0] + 1)
                if k == 0 and KT * h + part > 0:
                    pe.wait_ge(z_ready, KT * h + part)
                for q in range(GROUP):
                    s, side = BLOCKS[GROUP * g + q]
                    last = nc.tensor.matmul(zacc[32 * q:32 * q + 32, :], pick[:, 30 - 2 * k:62 - 2 * k],
                                            prod[:, (NS * h + s) % PRING, side, :],
                                            start=(k == 0), stop=(k == GROUPS_PER_KT - 1), skip_group_check=True)
                last.then_inc(groups_summed, 1)

            pe.wait_ge(ident_made, 1)
            pe.wait_ge(dense_in, 16)
            for h in range(HALVES):
                if h:
                    pe.wait_ge(dense_ready, h)
                for t in range(TILES):
                    last = nc.tensor.transpose(xps[0:DENSE, PART * t:PART * t + PART],
                                               dense_sb[:, TILES * h + t, :], ident[:, :])
                last.then_inc(dense_transposed, 1)
            transpose_level(0)
            pe.wait_ge(w_zeroed, 1)
            pe.wait_ge(pick_made, 2)

            for h in range(HALVES):
                for s, (m, mp) in enumerate(STEPS):
                    at = NS * h + s
                    if mp == m:
                        pe.wait_ge(x_ready, LEVELS * h + LEVELS - m)
                        if h == 0:
                            pe.wait_ge(w_in[m], 16 if m == LEVELS - 1 else 32)
                    if at >= LRING:
                        pe.wait_ge(prod_ready, at - LRING + 1)
                    if h and s < LRING:
                        pe.wait_ge(h2_ready, 2 * h)
                        pe.wait_ge(y_ready, h)
                    col = COL[(m, mp)]
                    for side in range(1 if mp == m else 2):
                        half = slice(DIM * side, DIM * side + DIM)
                        last = nc.tensor.matmul(left[:, at % LRING, side, :], Wsb[half, col:col + PART],
                                                xT[half, h, m, :], start=True, stop=True)
                    last.then_inc(left_ready, 1)
                    if transposes_after(m, mp) and LEVELS * h + LEVELS - m < LEVELS * HALVES:
                        transpose_level(LEVELS * h + LEVELS - m)
                    for g in groups_after(s):
                        sum_group(h, g)
                for g in groups_left():
                    sum_group(h, g)

                pe.wait_ge(prod_ready, NS * (h + 1))
                pe.wait_ge(z_ready, KT * (h + 1))
                if h == 0:
                    pe.wait_ge(w1_in, 16 * sum(2 if n else 1 for *_, n in runs))
                    pe.wait_ge(consts_in, 16 * 5)
                for o in range(HID1 // PART):
                    cols = slice(PART * o, PART * o + PART)
                    for k in range(KT):
                        nc.tensor.matmul(left[:, o // 2, o % 2, :], w1[:, k, cols], zT[:, k, :],
                                         start=(k == 0), stop=False)
                    nc.tensor.matmul(left[:, o // 2, o % 2, :], w1d[:, cols], denseT[:, h, :],
                                     start=False, stop=True).then_inc(h1_summed, 1)
                for o in range(HID2 // PART):
                    for k in range(HID1 // PART):
                        if o == 0:
                            pe.wait_ge(h1_ready, HID1 // PART * h + k + 1)
                        last = nc.tensor.matmul(left[:, 2, o, :], w2[:, k, PART * o:PART * o + PART], h1T[:, k, :],
                                                start=(k == 0), stop=(k == HID1 // PART - 1))
                    last.then_inc(h2_summed, 1)
                for k in range(HID2 // PART):
                    pe.wait_ge(h2_ready, HID2 // PART * h + k + 1)
                    last = nc.tensor.matmul(left[0:1, 0, 0, :], w3[:, k:k + 1], h2T[:, k, :],
                                            start=(k == 0), stop=(k == HID2 // PART - 1))
                last.then_inc(y_summed, 1)

        @block.vector
        def _(dve):
            nc.vector.memset(pick[:, :], 0.0).then_inc(pick_zeroed, 1)
            for m in range(LEVELS):
                last = nc.vector.memset(Wsb[0:DIM, COL[(m, m)]:COL[(m, m)] + DIM], 0.0)
            last.then_inc(w_zeroed, 1)
            nc.vector.memset(w1[:, :, :], 0.0).then_inc(w1_zeroed, 1)
            dve.wait_ge(pick_zeroed, 1)
            nc.vector.memset(pick[0:DIM, 30:31], 1.0).then_inc(pick_made, 1)
            nc.vector.memset(pick[DIM:PART, 31:32], 1.0).then_inc(pick_made, 1)
            for h in range(HALVES):
                for s, (m, mp) in enumerate(STEPS):
                    at = NS * h + s
                    dve.wait_ge(left_ready, at + 1)
                    if at >= PRING:
                        old = at - PRING
                        g = LAST_BLOCK_OF_STEP[old % NS] // GROUP
                        dve.wait_ge(groups_summed, GROUPS * (old // NS) + g + 1)
                    sides = 1 if mp == m else 2
                    xj = xT[:, h, mp, :].unsqueeze(1).broadcast_to([PART, sides, HALF])
                    nc.vector.tensor_tensor(prod[:, at % PRING, 0:sides, :], left[:, at % LRING, 0:sides, :],
                                            xj, ALU.mult).then_inc(prod_ready, 1)

        @block.scalar
        def _(act):
            for h in range(HALVES):
                act.wait_ge(dense_transposed, h + 1)
                nc.scalar.copy(denseT[:, h, :], xps[0:DENSE, :]).then_inc(dense_ready, 1)

            def copy_level(n):
                act.wait_ge(x_transposed, n + 1)
                nc.scalar.copy(xT[:, n // LEVELS, LEVELS - 1 - n % LEVELS, :], xps[:, :]).then_inc(x_ready, 1)

            def copy_part(h, g):
                if g % GROUPS_PER_KT == GROUPS_PER_KT - 1:
                    part = g // GROUPS_PER_KT
                    act.wait_ge(groups_summed, GROUPS * h + g + 1)
                    if h:
                        act.wait_ge(h1_summed, HID1 // PART * h)
                    nc.scalar.copy(zT[:, part, :], zacc[:, :]).then_inc(z_ready, 1)

            copy_level(0)
            for h in range(HALVES):
                for s, (m, mp) in enumerate(STEPS):
                    if transposes_after(m, mp) and LEVELS * h + LEVELS - m < LEVELS * HALVES:
                        copy_level(LEVELS * h + LEVELS - m)
                    for g in groups_after(s):
                        copy_part(h, g)
                for g in groups_left():
                    copy_part(h, g)
                act.wait_ge(consts_in, 16 * 5)
                for o in range(HID1 // PART):
                    act.wait_ge(h1_summed, HID1 // PART * h + o + 1)
                    if h:
                        act.wait_ge(h2_summed, HID2 // PART * h)
                    nc.scalar.activation(h1T[:, o, :], left[:, o // 2, o % 2, :], ACT.Relu,
                                         bias=b1[:, o:o + 1]).then_inc(h1_ready, 1)
                for o in range(HID2 // PART):
                    act.wait_ge(h2_summed, HID2 // PART * h + o + 1)
                    if h:
                        act.wait_ge(y_summed, h)
                    nc.scalar.activation(h2T[:, o, :], left[:, 2, o, :], ACT.Relu,
                                         bias=b2[:, o:o + 1]).then_inc(h2_ready, 1)
                act.wait_ge(y_summed, h + 1)
                nc.scalar.copy(ysb[0:1, h, :], left[0:1, 0, 0, :]).then_inc(y_ready, 1)


TABLES = [f"tbl_{f}" for f in range(FIELDS)]
INPUTS = ["dense_ctx", "ids", *TABLES, "W_top1", "b_top1", "W_top2", "b_top2", "W_top3", "L0_rec_W"]


def kernel(**inputs):
    import numpy as np
    import concourse.bacc as bacc
    from concourse.bass_utils import run_bass_kernel_spmd

    nc = bacc.Bacc("TRN2", target_bir_lowering=False, num_devices=1)
    arrays, aps = {}, {}
    for name in INPUTS:
        a = np.ascontiguousarray(inputs[name])
        arrays[f"in_{name}"] = a
        aps[name] = nc.dram_tensor(f"in_{name}", a.shape, mybir.dt.from_np(a.dtype), kind="ExternalInput").ap()
    y = nc.dram_tensor("out_y", (BATCH, 1), FP32, kind="ExternalOutput").ap()
    build(nc, aps["dense_ctx"], aps["ids"], [aps[t] for t in TABLES], aps["W_top1"], aps["b_top1"],
          aps["W_top2"], aps["b_top2"], aps["W_top3"], aps["L0_rec_W"], y)
    r = run_bass_kernel_spmd(nc, [arrays], core_ids=[0])
    return r.results[0]["out_y"]
```

```python
import concourse.bass as bass
from concourse import mybir
from contextlib import ExitStack

FP32 = mybir.dt.float32
INT32 = mybir.dt.int32
ALU = mybir.AluOpType
ACT = mybir.ActivationFunctionType

FP32R = mybir.dt.float32r

BATCH, FIELDS, DIM, DENSE = 1024, 32, 64, 16
PAIRS = FIELDS * (FIELDS - 1) // 2
HID1, HID2 = 512, 256
PART = 128
HALF = 512
HALVES = BATCH // HALF
TILES = BATCH // PART
LEVELS = FIELDS // 2
KT = 4
O1, O2 = HID1 // PART, HID2 // PART

TURNS = [[(i, m) for m in range((i + 1) // 2, LEVELS)] for i in reversed(range(FIELDS))]
FIRST = [sum(len(t) for t in TURNS[:n]) for n in range(FIELDS + 1)]
BLOCKS = [b for t in TURNS for b in t]
NB = len(BLOCKS)
GROUP = 4
GROUPS = NB // GROUP
GROUPS_PER_KT = GROUPS // KT
CHUNK = 4
LAG = 3
AHEAD = 4
LRING, PRING, ROWRING, XRING, RAWRING = 3, 8, 4, 3, 2


def pair_row(i, j):
    return i * (2 * FIELDS - i - 1) // 2 + j - i - 1


def chunks(n):
    return (len(TURNS[n]) + CHUNK - 1) // CHUNK


def weights_chunk(n, c, size=CHUNK):
    first = DIM * (n % 2) if c == 0 else PART * size * c
    return slice(first, PART * min(len(TURNS[n]), size * (c + 1)))


CHUNKS_BEFORE = [sum(chunks(k) for k in range(n)) for n in range(FIELDS + 1)]


def group_after(b):
    done = b - LAG
    return done // GROUP if done >= 0 and done % GROUP == GROUP - 1 else None


def prepared_after(n):
    late = max(0, len(TURNS[n]) - AHEAD)
    return max([k for k in range(late + 1) if group_after(FIRST[n] + k) is not None][-1:] or [late])


PREPARED_AFTER = [None] + [prepared_after(n) for n in range(1, FIELDS - 1)] + [None]


def ring_uses():
    u, of_field, of_block = 2, [0, 1], []
    for n, turn in enumerate(TURNS):
        for k in range(len(turn)):
            of_block.append(u)
            u += 1
            if k == PREPARED_AFTER[n]:
                of_field.append(u)
                u += 1
    return of_field, of_block, u


FIELD_USE, BLOCK_USE, TOP_USE = ring_uses()
USER = {**{u: ("field", n) for n, u in enumerate(FIELD_USE)}, **{u: ("block", b) for b, u in enumerate(BLOCK_USE)}}


def groups_left():
    return [g for g in range(GROUPS) if GROUP * g + GROUP - 1 + LAG >= NB]


def place(b):
    g = b // GROUP
    return g // GROUPS_PER_KT, 32 * (b % GROUP) + 2 * (g % GROUPS_PER_KT)


def top1_runs(n):
    runs = {}
    for b in range(FIRST[n], FIRST[n + 1]):
        i, m = BLOCKS[b]
        part, at = place(b)
        for two in range(2):
            if 2 * m + two > i:
                runs.setdefault((part, b % GROUP, two), []).append((at + two, pair_row(i, 2 * m + two)))
    return [(part, *rows[0], len(rows)) for (part, _, _), rows in runs.items()]


def build(nc, dense_ctx, ids, tables, W_top1, b_top1, W_top2, b_top2, W_top3, W, y):
    ctx = ExitStack()
    with ctx:
        def sb(name, shape, dt=FP32):
            return ctx.enter_context(nc.sbuf_tensor(name, shape, dt))

        def sem(name):
            return ctx.enter_context(nc.semaphore(name))

        ids_sb = sb("ids_sb", [PART, TILES, FIELDS], INT32)
        dense_sb = sb("dense_sb", [PART, TILES, DENSE])
        rows = sb("rows", [PART, ROWRING, TILES, 2, DIM])
        xT = sb("xT", [PART, LEVELS, BATCH])
        xsplit = sb("xsplit", [PART, XRING, 2, BATCH], FP32R)
        wraw = sb("wraw", [PART, RAWRING, LEVELS * PART])
        wsplit = sb("wsplit", [PART, 2, LEVELS * PART], FP32R)
        prod = sb("prod", [PART, PRING, BATCH])
        w1 = sb("w1", [PART, KT, HID1])
        w1d = sb("w1d", [DENSE, HID1])
        w2 = sb("w2", [PART, O1, HID2])
        w3 = sb("w3", [PART, O2])
        b1 = sb("b1", [PART, O1])
        b2 = sb("b2", [PART, O2])
        zT = sb("zT", [PART, KT, BATCH])
        denseT = sb("denseT", [DENSE, BATCH])
        ident = sb("ident", [PART, PART])
        pick = sb("pick", [PART, 62])
        h1T, h2T = xT[:, 0:O1, :], xT[:, O1:O1 + O2, :]
        ysb = xT[0:1, O1 + O2, :]

        ring = ctx.enter_context(nc.psum_tensor("ring", [PART, LRING, HALVES, HALF], FP32))
        zacc = ctx.enter_context(nc.psum_tensor("zacc", [PART, HALVES, HALF], FP32))

        ids_in = sem("ids_in")
        dense_in = sem("dense_in")
        consts_in = sem("consts_in")
        w1_in = sem("w1_in")
        w1_zeroed = sem("w1_zeroed")
        pads_zeroed = sem("pads_zeroed")
        w_in = [sem(f"w_in{r}") for r in range(RAWRING)]
        w_high = sem("w_high")
        w_low = sem("w_low")
        rows_in = [sem(f"rows_in{r}") for r in range(ROWRING)]
        ident_zeroed = sem("ident_zeroed")
        ident_made = sem("ident_made")
        pick_zeroed = sem("pick_zeroed")
        pick_made = sem("pick_made")
        rows_twice = sem("rows_twice")
        x_transposed = sem("x_transposed")
        x_high = sem("x_high")
        x_low = sem("x_low")
        x_ready = sem("x_ready")
        dense_transposed = sem("dense_transposed")
        dense_ready = sem("dense_ready")
        left_ready = sem("left_ready")
        prod_ready = sem("prod_ready")
        groups_summed = sem("groups_summed")
        z_ready = sem("z_ready")
        h1_summed = sem("h1_summed")
        h1_ready = sem("h1_ready")
        h2_summed = sem("h2_summed")
        h2_ready = sem("h2_ready")
        y_summed = sem("y_summed")
        y_ready = sem("y_ready")
        y_out = sem("y_out")

        W1_DMAS = sum(len(top1_runs(n)) for n in range(FIELDS))
        block = ctx.enter_context(nc.Block())

        @block.sync
        def _(sp):
            sp.dma_start(ids_sb[:, :, :], ids.rearrange("(t p) f -> p t f", p=PART)).then_inc(ids_in, 16)
            for n in range(1, FIELDS):
                i = FIELDS - 1 - n
                at = DIM * (1 - i % 2)
                old = n - RAWRING
                if old >= 1:
                    sp.wait_ge(w_low, CHUNKS_BEFORE[old + 1])
                for two in range(2):
                    sp.dma_start(
                        wraw[DIM * two:DIM * two + DIM, n % RAWRING, at:at + n * DIM].rearrange("d (p e) -> d p e", e=DIM),
                        W[pair_row(i, i + 1):pair_row(i, i + 1) + n, :, :].rearrange("p d e -> d p e"),
                    ).then_inc(w_in[n % RAWRING], 16)
                if n == 1:
                    sp.dma_start(dense_sb[:, :, :], dense_ctx.rearrange("(t p) k -> p t k", p=PART)).then_inc(dense_in, 16)
                    sp.wait_ge(w1_zeroed, 1)
                for part, partition, row, count in top1_runs(n):
                    sp.dma_start(w1[partition:partition + 2 * (count - 1) + 1:2, part, :],
                                 W_top1[row:row + 2 * GROUP * (count - 1) + 1:2 * GROUP, :]).then_inc(w1_in, 16)
            sp.dma_start(w1d[:, :], W_top1[PAIRS:PAIRS + DENSE, :]).then_inc(consts_in, 16)
            sp.dma_start(w2[:, :, :], W_top2.rearrange("(k p) n -> p k n", p=PART)).then_inc(consts_in, 16)
            sp.dma_start(w3[:, :], W_top3.rearrange("(k p) n -> p (k n)", p=PART),
                         allow_slow_non_contiguous=True).then_inc(consts_in, 16)
            sp.dma_start(b1[:, :], b_top1.rearrange("(k p) -> p k", p=PART),
                         allow_slow_non_contiguous=True).then_inc(consts_in, 16)
            sp.dma_start(b2[:, :], b_top2.rearrange("(k p) -> p k", p=PART),
                         allow_slow_non_contiguous=True).then_inc(consts_in, 16)
            sp.wait_ge(y_ready, 1)
            sp.dma_start(y.rearrange("b n -> n b"), ysb).then_inc(y_out, 16)
            sp.wait_ge(y_out, 16)

        @block.gpsimd
        def _(pool):
            nc.gpsimd.memset(ident[:, :], 0.0).then_inc(ident_zeroed, 1)
            pool.wait_ge(ident_zeroed, 1)
            nc.gpsimd.affine_select(out=ident[:, :], in_=ident[:, :], compare_op=ALU.not_equal, fill=1.0,
                                    base=0, pattern=[[-1, PART]], channel_multiplier=1).then_inc(ident_made, 1)
            pool.wait_ge(ids_in, 16)
            for n in range(FIELDS):
                f = FIELDS - 1 - n
                if n >= ROWRING:
                    pool.wait_ge(x_transposed, n - ROWRING + 1)
                for t in range(TILES):
                    nc.gpsimd.indirect_dma_start(
                        rows[:, n % ROWRING, t, 0, :], None, tables[f][:, :],
                        bass.IndirectOffsetOnAxis(ap=ids_sb[:, t, f:f + 1], axis=0),
                    ).then_inc(rows_in[n % ROWRING], 16)

        @block.tensor
        def _(pe):
            def wait_ring(u):
                if u < LRING:
                    return
                kind, k = USER[u - LRING]
                if kind == "block":
                    pe.wait_ge(prod_ready, k + 1)
                else:
                    pe.wait_ge(x_low, k + 1)
                    pe.wait_ge(x_ready, k + 1)

            def transpose_field(n):
                u = FIELD_USE[n]
                pe.wait_ge(rows_twice, n + 1)
                wait_ring(u)
                for t in range(TILES):
                    at = PART * (t % (TILES // HALVES))
                    last = nc.tensor.transpose(ring[:, u % LRING, t // (TILES // HALVES), at:at + PART],
                                               rows[:, n % ROWRING, t, :, :].rearrange("p a d -> p (a d)"), ident[:, :])
                last.then_inc(x_transposed, 1)

            def sum_group(g):
                part, k = g // GROUPS_PER_KT, g % GROUPS_PER_KT
                pe.wait_ge(prod_ready, GROUP * g + GROUP)
                if k == 0 and part > 0:
                    pe.wait_ge(z_ready, part)
                for h in range(HALVES):
                    for q in range(GROUP):
                        last = nc.tensor.matmul(zacc[32 * q:32 * q + 32, h, :], pick[:, 30 - 2 * k:62 - 2 * k],
                                                prod[:, (GROUP * g + q) % PRING, HALF * h:HALF * h + HALF],
                                                start=(k == 0), stop=(k == GROUPS_PER_KT - 1), skip_group_check=True)
                last.then_inc(groups_summed, 1)

            pe.wait_ge(ident_made, 1)
            pe.wait_ge(dense_in, 16)
            for t in range(TILES):
                at = PART * (t % (TILES // HALVES))
                last = nc.tensor.transpose(zacc[0:DENSE, t // (TILES // HALVES), at:at + PART], dense_sb[:, t, :], ident[:, :])
            last.then_inc(dense_transposed, 1)
            transpose_field(0)
            transpose_field(1)
            pe.wait_ge(dense_ready, 1)
            pe.wait_ge(pads_zeroed, 1)
            pe.wait_ge(pick_made, 2)

            for n, turn in enumerate(TURNS):
                if turn:
                    pe.wait_ge(x_low, n + 1)
                for k in range(len(turn)):
                    b = FIRST[n] + k
                    u = BLOCK_USE[b]
                    if k % CHUNK == 0:
                        pe.wait_ge(w_low, CHUNKS_BEFORE[n] + k // CHUNK + 1)
                    wait_ring(u)
                    for part in range(2):
                        for h in range(HALVES):
                            last = nc.tensor.matmul(ring[:, u % LRING, h, :], wsplit[:, n % 2, PART * k:PART * k + PART],
                                                    xsplit[:, n % XRING, 1 - part, HALF * h:HALF * h + HALF],
                                                    start=(part == 0), stop=(part == 1))
                    last.then_inc(left_ready, 1)
                    if k == PREPARED_AFTER[n]:
                        transpose_field(n + 1)
                    g = group_after(b)
                    if g is not None:
                        sum_group(g)
            for g in groups_left():
                sum_group(g)

            pe.wait_ge(prod_ready, NB)
            pe.wait_ge(w1_in, 16 * W1_DMAS)
            pe.wait_ge(consts_in, 16 * 5)
            for o in range(O1):
                cols = slice(PART * o, PART * o + PART)
                if o >= LRING:
                    pe.wait_ge(h1_ready, o - LRING + 1)
                for h in range(HALVES):
                    at = slice(HALF * h, HALF * h + HALF)
                    nc.tensor.matmul(ring[:, o % LRING, h, :], w1d[:, cols], denseT[:, at], start=True, stop=False)
                    for k in range(KT):
                        if o == 0 and h == 0:
                            pe.wait_ge(z_ready, k + 1)
                        last = nc.tensor.matmul(ring[:, o % LRING, h, :], w1[:, k, cols], zT[:, k, at],
                                                start=False, stop=(k == KT - 1))
                last.then_inc(h1_summed, 1)
            for o in range(O2):
                for h in range(HALVES):
                    for k in range(O1):
                        if o == 0 and h == 0:
                            pe.wait_ge(h1_ready, max(k, 1) + 1)
                        last = nc.tensor.matmul(ring[:, (O1 + o) % LRING, h, :], w2[:, k, PART * o:PART * o + PART],
                                                h1T[:, k, HALF * h:HALF * h + HALF], start=(k == 0), stop=(k == O1 - 1))
                last.then_inc(h2_summed, 1)
            for k in range(O2):
                pe.wait_ge(h2_ready, k + 1)
                for h in range(HALVES):
                    last = nc.tensor.matmul(ring[0:1, (O1 + O2) % LRING, h, :], w3[:, k:k + 1],
                                            h2T[:, k, HALF * h:HALF * h + HALF], start=(k == 0), stop=(k == O2 - 1))
            last.then_inc(y_summed, 1)

        @block.vector
        def _(dve):
            nc.vector.memset(pick[:, :], 0.0).then_inc(pick_zeroed, 1)
            nc.vector.memset(wsplit[:, 1, 0:DIM].bitcast(FP32), 0.0).then_inc(pads_zeroed, 1)
            nc.vector.memset(w1[:, :, :], 0.0).then_inc(w1_zeroed, 1)
            dve.wait_ge(pick_zeroed, 1)
            nc.vector.memset(pick[0:DIM, 30:31], 1.0).then_inc(pick_made, 1)
            nc.vector.memset(pick[DIM:PART, 31:32], 1.0).then_inc(pick_made, 1)

            def weights_low(n, c):
                dve.wait_ge(w_high, n)
                cols = weights_chunk(n, c)
                nc.vector.tensor_tensor(wsplit[DIM:PART, n % 2, cols], wraw[DIM:PART, n % RAWRING, cols],
                                        wsplit[DIM:PART, n % 2, cols].bitcast(FP32), ALU.subtract).then_inc(w_low, 1)

            def field_low(n):
                dve.wait_ge(x_high, n + 1)
                dve.wait_ge(x_ready, n + 1)
                u = FIELD_USE[n]
                nc.vector.tensor_tensor(xsplit[:, n % XRING, 1, :], ring[:, u % LRING, :, :].rearrange("p h c -> p (h c)"),
                                        xsplit[:, n % XRING, 0, :].bitcast(FP32), ALU.subtract).then_inc(x_low, 1)

            weights_low(1, 0)
            field_low(0)
            field_low(1)
            for n, turn in enumerate(TURNS):
                for k, (i, m) in enumerate(turn):
                    b = FIRST[n] + k
                    u = BLOCK_USE[b]
                    dve.wait_ge(left_ready, b + 1)
                    if k == 0:
                        dve.wait_ge(x_ready, n + 1)
                    if b >= PRING:
                        dve.wait_ge(groups_summed, (b - PRING) // GROUP + 1)
                    nc.vector.tensor_tensor(prod[:, b % PRING, :], ring[:, u % LRING, :, :].rearrange("p h c -> p (h c)"),
                                            xT[:, m, :], ALU.mult).then_inc(prod_ready, 1)
                    if n + 1 < FIELDS:
                        for c in range(chunks(n + 1)):
                            if k == min(CHUNK * c, len(turn) - 1):
                                weights_low(n + 1, c)
                    if k == PREPARED_AFTER[n]:
                        field_low(n + 1)

        @block.scalar
        def _(act):
            def copy_rows(n):
                act.wait_ge(rows_in[n % ROWRING], 16 * TILES * (n // ROWRING + 1))
                nc.scalar.copy(rows[:, n % ROWRING, :, 1, :], rows[:, n % ROWRING, :, 0, :]).then_inc(rows_twice, 1)

            def copy_field(n):
                u = FIELD_USE[n]
                act.wait_ge(x_transposed, n + 1)
                if n >= XRING:
                    act.wait_ge(left_ready, FIRST[n - XRING + 1])
                flat = ring[:, u % LRING, :, :].rearrange("p h c -> p (h c)")
                nc.scalar.copy(xsplit[:, n % XRING, 0, :], flat).then_inc(x_high, 1)
                f = FIELDS - 1 - n
                half = slice(DIM * (f % 2), DIM * (f % 2) + DIM)
                nc.scalar.copy(xT[half, f // 2, :], flat[half, :]).then_inc(x_ready, 1)

            def weights_high(n):
                i = FIELDS - 1 - n
                act.wait_ge(w_in[n % RAWRING], 32 * ((n - 1) // RAWRING + 1))
                if n > 2:
                    act.wait_ge(left_ready, FIRST[n - 1])
                cols = slice(DIM * (1 - i % 2), PART * len(TURNS[n]))
                nc.scalar.copy(wsplit[:, n % 2, cols], wraw[:, n % RAWRING, cols]).then_inc(w_high, 1)

            def copy_part(g):
                part = g // GROUPS_PER_KT
                act.wait_ge(groups_summed, g + 1)
                nc.scalar.copy(zT[:, part, :], zacc[:, :, :].rearrange("p h c -> p (h c)")).then_inc(z_ready, 1)

            weights_high(1)
            act.wait_ge(dense_transposed, 1)
            nc.scalar.copy(denseT[:, :], zacc[0:DENSE, :, :].rearrange("p h c -> p (h c)")).then_inc(dense_ready, 1)
            copy_rows(0)
            copy_field(0)
            copy_rows(1)
            copy_field(1)
            for n, turn in enumerate(TURNS):
                if turn and n + 1 < FIELDS:
                    weights_high(n + 1)
                    copy_rows(n + 1)
                for k in range(len(turn)):
                    if k == PREPARED_AFTER[n]:
                        copy_field(n + 1)
                    g = group_after(FIRST[n] + k)
                    if g is not None and g % GROUPS_PER_KT == GROUPS_PER_KT - 1:
                        copy_part(g)
            copy_part(GROUPS - 1)

            act.wait_ge(consts_in, 16 * 5)
            for o in range(O1):
                act.wait_ge(h1_summed, o + 1)
                nc.scalar.activation(h1T[:, o, :], ring[:, o % LRING, :, :].rearrange("p h c -> p (h c)"), ACT.Relu,
                                     bias=b1[:, o:o + 1]).then_inc(h1_ready, 1)
            for o in range(O2):
                act.wait_ge(h2_summed, o + 1)
                nc.scalar.activation(h2T[:, o, :], ring[:, (O1 + o) % LRING, :, :].rearrange("p h c -> p (h c)"), ACT.Relu,
                                     bias=b2[:, o:o + 1]).then_inc(h2_ready, 1)
            act.wait_ge(y_summed, 1)
            nc.scalar.copy(ysb, ring[0:1, (O1 + O2) % LRING, :, :].rearrange("p h c -> p (h c)")).then_inc(y_ready, 1)


TABLES = [f"tbl_{f}" for f in range(FIELDS)]
INPUTS = ["dense_ctx", "ids", *TABLES, "W_top1", "b_top1", "W_top2", "b_top2", "W_top3", "L0_rec_W"]


def kernel(**inputs):
    import numpy as np
    import concourse.bacc as bacc
    from concourse.bass_utils import run_bass_kernel_spmd

    nc = bacc.Bacc("TRN2", target_bir_lowering=False, num_devices=1)
    arrays, aps = {}, {}
    for name in INPUTS:
        a = np.ascontiguousarray(inputs[name])
        arrays[f"in_{name}"] = a
        aps[name] = nc.dram_tensor(f"in_{name}", a.shape, mybir.dt.from_np(a.dtype), kind="ExternalInput").ap()
    y = nc.dram_tensor("out_y", (BATCH, 1), FP32, kind="ExternalOutput").ap()
    build(nc, aps["dense_ctx"], aps["ids"], [aps[t] for t in TABLES], aps["W_top1"], aps["b_top1"],
          aps["W_top2"], aps["b_top2"], aps["W_top3"], aps["L0_rec_W"], y)
    r = run_bass_kernel_spmd(nc, [arrays], core_ids=[0])
    return r.results[0]["out_y"]
```

```python
import concourse.bass as bass
from concourse import mybir
from contextlib import ExitStack

FP32 = mybir.dt.float32
INT32 = mybir.dt.int32
ALU = mybir.AluOpType
ACT = mybir.ActivationFunctionType

FP32R = mybir.dt.float32r

BATCH, FIELDS, DIM, DENSE = 1024, 32, 64, 16
PAIRS = FIELDS * (FIELDS - 1) // 2
HID1, HID2 = 512, 256
PART = 128
HALF = 512
HALVES = BATCH // HALF
TILES = BATCH // PART
LEVELS = FIELDS // 2
O1, O2 = HID1 // PART, HID2 // PART

TURNS = [[(i, m) for m in range((i + 1) // 2, LEVELS)] for i in reversed(range(FIELDS))]
FIRST = [sum(len(t) for t in TURNS[:n]) for n in range(FIELDS + 1)]
BLOCKS = [b for t in TURNS for b in t]
NB = len(BLOCKS)


def is_half(b):
    return BLOCKS[b][0] == 2 * BLOCKS[b][1]


SLAB_BLOCKS = [[b] if not is_half(b) else [BLOCKS.index((i + 2, m + 1)), b]
               for b, (i, m) in enumerate(BLOCKS) if not (is_half(b) and m % 2)]
SLAB = {b: s for s, blocks in enumerate(SLAB_BLOCKS) for b in blocks}
SLABS = len(SLAB_BLOCKS)
FULL = [b for b in range(NB) if not is_half(b)]
HALF_BLOCKS = [b for b in range(NB) if is_half(b)]
GROUP = 4
GROUPS = SLABS // GROUP
KT = 4
GROUPS_PER_KT = 16
DENSE_AT = 2 * (GROUPS - (KT - 1) * GROUPS_PER_KT)
DENSE_Q = 32 - DENSE_AT
DENSE_GROUP = GROUPS - 4
HALF_RING = 2
CHUNK = 4
LAG = 3
POOL_FROM = 16
AHEAD = 3
LRING, PRING, ROWRING, XRING, RAWRING = 3, 7, 4, 3, 2

AT_ONCE = 3
TWO_AHEAD = 7
LOOKED = 4
TABLE_PARTS = 8
EARLY = 0
ONEHOTS = 4


def pair_row(i, j):
    return i * (2 * FIELDS - i - 1) // 2 + j - i - 1


def chunks(n):
    return (len(TURNS[n]) + CHUNK - 1) // CHUNK


def weights_chunk(n, c, size=CHUNK):
    first = DIM * (n % 2) if c == 0 else PART * size * c
    return slice(first, PART * min(len(TURNS[n]), size * (c + 1)))


CHUNKS_BEFORE = [sum(chunks(k) for k in range(n)) for n in range(FIELDS + 1)]


LAST_BLOCK = [max(b for slab in SLAB_BLOCKS[GROUP * g:GROUP * g + GROUP] for b in slab) for g in range(GROUPS)]


def group_after(b):
    return LAST_BLOCK.index(b - LAG) if b - LAG in LAST_BLOCK else None


def field_after(n):
    fields = [f for f in range(AT_ONCE, FIELDS) if n == (f - 2 if f <= TWO_AHEAD else f - 1)]
    if not fields:
        return None, None
    late = max(0, len(TURNS[n]) - AHEAD)
    return fields[0], max([k for k in range(late + 1) if group_after(FIRST[n] + k) is not None][-1:] or [late])


FIELD_IN, PREPARED_AFTER = zip(*[field_after(n) for n in range(FIELDS)])


def ring_uses():
    u, of_field, of_block = LOOKED + AT_ONCE, [LOOKED + n for n in range(AT_ONCE)], []
    for n, turn in enumerate(TURNS):
        for k in range(len(turn)):
            of_block.append(u)
            u += 1
            if k == PREPARED_AFTER[n]:
                of_field.append(u)
                u += 1
    return of_field, of_block, u


FIELD_USE, BLOCK_USE, TOP_USE = ring_uses()
USER = {**{u: ("field", n) for n, u in enumerate(FIELD_USE)}, **{u: ("block", b) for b, u in enumerate(BLOCK_USE)},
        **{u: ("ids", u) for u in range(LOOKED)}}


def groups_left():
    return [g for g in range(GROUPS) if LAST_BLOCK[g] + LAG >= NB]


def closes_part(g):
    return g % GROUPS_PER_KT == GROUPS_PER_KT - 1 or g == GROUPS - 1


def top1_runs(n):
    runs = {}
    for b in range(FIRST[n], FIRST[n + 1]):
        i, m = BLOCKS[b]
        g, q = SLAB[b] // GROUP, SLAB[b] % GROUP
        part, at = g // GROUPS_PER_KT, 32 * q + 2 * (g % GROUPS_PER_KT)
        if is_half(b) and m % 2:
            runs["half"] = [(part, at, pair_row(i, i + 1))]
        else:
            for two in range(1 if is_half(b) else 0, 2):
                runs.setdefault((part, q, two), []).append((part, at + two, pair_row(i, 2 * m + two)))
    return [(*rows[0], len(rows)) for rows in runs.values()]


def build(nc, dense_ctx, ids, tables, W_top1, b_top1, W_top2, b_top2, W_top3, W, y):
    ctx = ExitStack()
    with ctx:
        def sb(name, shape, dt=FP32):
            return ctx.enter_context(nc.sbuf_tensor(name, shape, dt))

        def sem(name):
            return ctx.enter_context(nc.semaphore(name))

        with ExitStack() as early:
            ids_wide = early.enter_context(nc.sbuf_tensor("ids_wide", [PART, LOOKED, BATCH], FP32))
            table_raw = early.enter_context(nc.sbuf_tensor("table_raw", [PART, LOOKED, TABLE_PARTS, DIM], FP32))
            table_split = early.enter_context(nc.sbuf_tensor("table_split", [PART, LOOKED, TABLE_PARTS, 2, DIM], FP32R))
            onehot = early.enter_context(nc.sbuf_tensor("onehot", [PART, ONEHOTS, BATCH], FP32R))
        zT = sb("zT", [PART, KT, BATCH])
        xT = sb("xT", [PART, LEVELS, BATCH])
        ids_sb = sb("ids_sb", [PART, TILES, FIELDS], INT32)
        dense_sb = sb("dense_sb", [PART, TILES, DENSE])
        rows = sb("rows", [PART, ROWRING, TILES, 2, DIM])
        xsplit = sb("xsplit", [PART, XRING, 2, BATCH], FP32R)
        wraw = sb("wraw", [PART, RAWRING, LEVELS * PART])
        wsplit = sb("wsplit", [PART, 2, LEVELS * PART], FP32R)
        prod = sb("prod", [PART, PRING, BATCH])
        half_prod = sb("half_prod", [PART, HALF_RING, BATCH])
        w1 = sb("w1", [PART, KT, HID1])
        w2 = sb("w2", [PART, O1, HID2])
        w3 = sb("w3", [PART, O2])
        b1 = sb("b1", [PART, O1])
        b2 = sb("b2", [PART, O2])
        ident = sb("ident", [PART, PART])
        pick = sb("pick", [PART, 62])
        TABLE_PART = tables[FIELDS - 1].shape[0] // TABLE_PARTS
        assert all(tables[FIELDS - 1 - n].shape[0] == TABLE_PARTS * TABLE_PART for n in range(LOOKED)) and TABLE_PART <= PART
        ids_f = sb("ids_f", [PART, TILES, LOOKED])
        table_row = sb("table_row", [PART, TABLE_PARTS], INT32)
        table_row_f = sb("table_row_f", [PART, TABLE_PARTS])
        dense_placed = rows[:, (FIELDS - LOOKED) % ROWRING, :, :, :].rearrange("p t a d -> p t (a d)")
        h1T, h2T = xT[:, 0:O1, :], xT[:, O1:O1 + O2, :]
        ysb = xT[0:1, O1 + O2, :]

        ring = ctx.enter_context(nc.psum_tensor("ring", [PART, LRING, HALVES, HALF], FP32))
        zacc = ctx.enter_context(nc.psum_tensor("zacc", [PART, HALVES, HALF], FP32))

        ids_in = sem("ids_in")
        dense_in = sem("dense_in")
        consts_in = sem("consts_in")
        w1_in = sem("w1_in")
        w_in = [sem(f"w_in{r}") for r in range(RAWRING)]
        w_high = sem("w_high")
        w_low = sem("w_low")
        tables_in = [sem(f"tables_in{n}") for n in range(LOOKED)]
        rows_numbered = sem("rows_numbered")
        numbers_ready = sem("numbers_ready")
        ids_spread = sem("ids_spread")
        ids_wide_ready = sem("ids_wide_ready")
        table_high = sem("table_high")
        table_low = sem("table_low")
        onehot_ready = sem("onehot_ready")
        onehot_used = sem("onehot_used")
        w_low_pool = sem("w_low_pool")
        rows_in = [sem(f"rows_in{r}") for r in range(ROWRING)]
        ident_zeroed = sem("ident_zeroed")
        ident_made = sem("ident_made")
        pick_zeroed = sem("pick_zeroed")
        pick_made = sem("pick_made")
        rows_twice = sem("rows_twice")
        x_transposed = sem("x_transposed")
        x_high = sem("x_high")
        x_low = sem("x_low")
        x_ready = sem("x_ready")
        pads_zeroed = sem("pads_zeroed")
        dense_zeroed = sem("dense_zeroed")
        dense_ready = sem("dense_ready")
        left_ready = sem("left_ready")
        prod_ready = sem("prod_ready")
        groups_summed = sem("groups_summed")
        z_ready = sem("z_ready")
        h1_summed = sem("h1_summed")
        h1_ready = sem("h1_ready")
        h2_summed = sem("h2_summed")
        h2_ready = sem("h2_ready")
        y_summed = sem("y_summed")
        y_ready = sem("y_ready")
        y_out = sem("y_out")

        W1_DMAS = sum(len(top1_runs(n)) for n in range(FIELDS)) + GROUP
        def slab(b):
            return half_prod[:, HALF_BLOCKS.index(b) // 2 % HALF_RING, :] if is_half(b) else prod[:, FULL.index(b) % PRING, :]

        def y_columns(h):
            return ysb.rearrange("o (p t) -> o t p", t=TILES)[:, TILES // HALVES * h:TILES // HALVES * (h + 1), :]

        def side(n):
            f = FIELDS - 1 - n
            return slice(DIM * (f % 2), DIM * (f % 2) + DIM)

        def field_ready(engine, n):
            engine.wait_ge(x_low, n + 1)
            if n >= LOOKED:
                engine.wait_ge(x_ready, n - LOOKED + 1)

        block = ctx.enter_context(nc.Block())

        @block.sync
        def _(sp):
            sp.dma_start(ids_sb[:, :, :], ids.rearrange("(p t) f -> p t f", p=PART)).then_inc(ids_in, 16)
            for n in range(LOOKED):
                sp.dma_start(table_raw[0:TABLE_PART, n], tables[FIELDS - 1 - n].rearrange("(p k) d -> p k d", k=TABLE_PARTS)
                             ).then_inc(tables_in[n], 16)
            for n in range(1, FIELDS):
                i = FIELDS - 1 - n
                at = DIM * (1 - i % 2)
                old = n - RAWRING
                if old >= POOL_FROM:
                    sp.wait_ge(w_low_pool, old - POOL_FROM + 1)
                elif old >= 1:
                    sp.wait_ge(w_low, CHUNKS_BEFORE[old + 1])
                for two in range(2):
                    sp.dma_start(
                        wraw[DIM * two:DIM * two + DIM, n % RAWRING, at:at + n * DIM].rearrange("d (p e) -> d p e", e=DIM),
                        W[pair_row(i, i + 1):pair_row(i, i + 1) + n, :, :].rearrange("p d e -> d p e"),
                    ).then_inc(w_in[n % RAWRING], 16)
                if n == 1:
                    sp.dma_start(dense_sb[:, :, :], dense_ctx.rearrange("(p t) k -> p t k", p=PART)).then_inc(dense_in, 16)
                for part, partition, row, count in top1_runs(n):
                    sp.dma_start(w1[partition:partition + 2 * (count - 1) + 1:2, part, :],
                                 W_top1[row:row + 2 * GROUP * (count - 1) + 1:2 * GROUP, :]).then_inc(w1_in, 16)
            for q in range(GROUP):
                sp.dma_start(w1[32 * q + DENSE_AT:32 * q + 32, KT - 1, :],
                             W_top1[PAIRS + DENSE_Q * q:PAIRS + DENSE_Q * (q + 1), :]).then_inc(w1_in, 16)
            sp.dma_start(w2[:, :, :], W_top2.rearrange("(k p) n -> p k n", p=PART)).then_inc(consts_in, 16)
            sp.dma_start(w3[:, :], W_top3.rearrange("(k p) n -> p (k n)", p=PART),
                         allow_slow_non_contiguous=True).then_inc(consts_in, 16)
            sp.dma_start(b1[:, :], b_top1.rearrange("(k p) -> p k", p=PART),
                         allow_slow_non_contiguous=True).then_inc(consts_in, 16)
            sp.dma_start(b2[:, :], b_top2.rearrange("(k p) -> p k", p=PART),
                         allow_slow_non_contiguous=True).then_inc(consts_in, 16)
            sp.wait_ge(y_ready, HALVES)
            sp.dma_start(y.rearrange("b n -> n b"), ysb).then_inc(y_out, 16)
            sp.wait_ge(y_out, 16)

        @block.gpsimd
        def _(pool):
            nc.gpsimd.memset(ident[:, :], 0.0).then_inc(ident_zeroed, 1)
            pool.wait_ge(ident_zeroed, 1)
            nc.gpsimd.affine_select(out=ident[:, :], in_=ident[:, :], compare_op=ALU.not_equal, fill=1.0,
                                    base=0, pattern=[[-1, PART]], channel_multiplier=1).then_inc(ident_made, 1)
            nc.gpsimd.iota(table_row[:, :], pattern=[[1, TABLE_PARTS]], base=0,
                           channel_multiplier=TABLE_PARTS).then_inc(rows_numbered, 1)
            pool.wait_ge(ids_in, 16)
            def gathered(g):
                pool.wait_ge(rows_in[g % ROWRING], 16 * TILES * (g // ROWRING + 1))

            def weights_low(n):
                pool.wait_ge(w_high, n)
                cols = weights_chunk(n, 0, LEVELS)
                nc.gpsimd.tensor_tensor(wsplit[DIM:PART, n % 2, cols], wraw[DIM:PART, n % RAWRING, cols],
                                        wsplit[DIM:PART, n % 2, cols].bitcast(FP32), ALU.subtract).then_inc(w_low_pool, 1)
                pool.wait_ge(w_low_pool, n - POOL_FROM + 1)

            for g in range(FIELDS - LOOKED):
                f = FIELDS - 1 - LOOKED - g
                if g + LOOKED - 4 >= POOL_FROM:
                    gathered(g - 1)
                    weights_low(g + LOOKED - 4)
                if g >= ROWRING:
                    pool.wait_ge(x_transposed, g - ROWRING + 1)
                for t in range(TILES):
                    nc.gpsimd.indirect_dma_start(
                        rows[:, g % ROWRING, t, 0, :], None, tables[f][:, :],
                        bass.IndirectOffsetOnAxis(ap=ids_sb[:, t, f:f + 1], axis=0),
                    ).then_inc(rows_in[g % ROWRING], 16)
            gathered(FIELDS - LOOKED - 1)
            for n in range(FIELDS - 4, FIELDS):
                weights_low(n)
                if n == FIELDS - 2:
                    pool.wait_ge(x_transposed, FIELDS - LOOKED - ROWRING + 1)
                    nc.gpsimd.memset(dense_placed, 0.0).then_inc(dense_zeroed, 1)
                    pool.wait_ge(dense_zeroed, 1)
                    pool.wait_ge(dense_in, 16)
                    for q in range(GROUP):
                        nc.gpsimd.tensor_copy(dense_placed[:, :, 32 * q + DENSE_AT:32 * q + 32],
                                              dense_sb[:, :, DENSE_Q * q:DENSE_Q * (q + 1)]).then_inc(dense_ready, 1)
                    pool.wait_ge(dense_ready, GROUP)

        @block.tensor
        def _(pe):
            def wait_ring(u):
                if u < LRING:
                    return
                kind, k = USER[u - LRING]
                if kind == "block":
                    pe.wait_ge(prod_ready, k + 1)
                elif kind == "ids":
                    pe.wait_ge(ids_wide_ready, k + 1)
                else:
                    field_ready(pe, k)

            def transpose_field(n):
                u = FIELD_USE[n]
                pe.wait_ge(rows_twice, n - LOOKED + 1)
                wait_ring(u)
                for t in range(TILES):
                    at = PART * (t % (TILES // HALVES))
                    last = nc.tensor.transpose(ring[:, u % LRING, t // (TILES // HALVES), at:at + PART],
                                               rows[:, (n - LOOKED) % ROWRING, t, :, :].rearrange("p a d -> p (a d)"), ident[:, :])
                last.then_inc(x_transposed, 1)

            def spread_ids(n):
                wait_ring(n)
                for t in range(TILES):
                    at = PART * (t % (TILES // HALVES))
                    last = nc.tensor.matmul(ring[:, n % LRING, t // (TILES // HALVES), at:at + PART],
                                            ids_f[:, t, LOOKED - 1 - n:LOOKED - n].broadcast_to([PART, PART]), ident[:, :], start=True, stop=True)
                last.then_inc(ids_spread, 1)

            def look_up_field(n):
                u = FIELD_USE[n]
                wait_ring(u)
                pe.wait_ge(table_low, n + 1)
                for k in range(TABLE_PARTS):
                    o = n * TABLE_PARTS + k
                    pe.wait_ge(onehot_ready, o + 1)
                    for h in range(HALVES):
                        last = nc.tensor.matmul(ring[:, u % LRING, h, :],
                                                table_split[0:TABLE_PART, n, k, :, :].rearrange("p a d -> p (a d)"),
                                                onehot[0:TABLE_PART, o % ONEHOTS, HALF * h:HALF * h + HALF],
                                                start=(k == 0), stop=(k == TABLE_PARTS - 1))
                    last.then_inc(onehot_used, 1)

            def lay_out_field(n):
                if n < LOOKED:
                    look_up_field(n)
                else:
                    transpose_field(n)

            def sum_group(g):
                part, k = g // GROUPS_PER_KT, g % GROUPS_PER_KT
                pe.wait_ge(prod_ready, LAST_BLOCK[g] + 1)
                if k == 0 and part > 0:
                    pe.wait_ge(z_ready, part)
                if g == DENSE_GROUP:
                    pe.wait_ge(dense_ready, GROUP)
                    for t in range(TILES):
                        at = PART * (t % (TILES // HALVES))
                        nc.tensor.matmul(zacc[:, t // (TILES // HALVES), at:at + PART], dense_placed[:, t, :], ident[:, :],
                                         start=False, stop=False, skip_group_check=True)
                for h in range(HALVES):
                    for q in range(GROUP):
                        last = nc.tensor.matmul(zacc[32 * q:32 * q + 32, h, :], pick[:, 30 - 2 * k:62 - 2 * k],
                                                slab(SLAB_BLOCKS[GROUP * g + q][-1])[:, HALF * h:HALF * h + HALF],
                                                start=(k == 0), stop=closes_part(g), skip_group_check=True)
                last.then_inc(groups_summed, 1)

            pe.wait_ge(ident_made, 1)
            pe.wait_ge(numbers_ready, 1)
            for n in range(LOOKED):
                spread_ids(n)
            for n in range(AT_ONCE):
                lay_out_field(n)
            pe.wait_ge(pick_made, 2)
            pe.wait_ge(pads_zeroed, 1)

            for n, turn in enumerate(TURNS):
                if turn:
                    pe.wait_ge(x_low, n + 1)
                for k in range(len(turn)):
                    b = FIRST[n] + k
                    u = BLOCK_USE[b]
                    if n >= POOL_FROM and k == 0:
                        pe.wait_ge(w_low_pool, n - POOL_FROM + 1)
                    if n < POOL_FROM and k % CHUNK == 0:
                        pe.wait_ge(w_low, CHUNKS_BEFORE[n] + k // CHUNK + 1)
                    wait_ring(u)
                    for part in range(2):
                        for h in range(HALVES):
                            last = nc.tensor.matmul(ring[:, u % LRING, h, :], wsplit[:, n % 2, PART * k:PART * k + PART],
                                                    xsplit[:, n % XRING, 1 - part, HALF * h:HALF * h + HALF],
                                                    start=(part == 0), stop=(part == 1))
                    last.then_inc(left_ready, 1)
                    if k == PREPARED_AFTER[n]:
                        lay_out_field(FIELD_IN[n])
                    g = group_after(b)
                    if g is not None:
                        sum_group(g)
            for g in groups_left():
                sum_group(g)

            pe.wait_ge(prod_ready, NB)
            pe.wait_ge(w1_in, 16 * W1_DMAS)
            pe.wait_ge(consts_in, 16 * 4)
            for o in range(O1):
                cols = slice(PART * o, PART * o + PART)
                if o >= LRING:
                    pe.wait_ge(h1_ready, o - LRING + 1)
                for h in range(HALVES):
                    at = slice(HALF * h, HALF * h + HALF)
                    for k in range(KT):
                        if o == 0 and h == 0:
                            pe.wait_ge(z_ready, k + 1)
                        last = nc.tensor.matmul(ring[:, o % LRING, h, :], w1[:, k, cols], zT[:, k, at],
                                                start=(k == 0), stop=(k == KT - 1))
                last.then_inc(h1_summed, 1)
            for o in range(O2):
                for h in range(HALVES):
                    for k in range(O1):
                        if o == 0 and h == 0:
                            pe.wait_ge(h1_ready, max(k, 1) + 1)
                        last = nc.tensor.matmul(ring[:, (O1 + o) % LRING, h, :], w2[:, k, PART * o:PART * o + PART],
                                                h1T[:, k, HALF * h:HALF * h + HALF], start=(k == 0), stop=(k == O1 - 1))
                last.then_inc(h2_summed, 1)
            for k in range(O2):
                pe.wait_ge(h2_ready, k + 1)
                for h in range(HALVES):
                    last = nc.tensor.matmul(ring[32 * h:32 * h + 1, (O1 + O2) % LRING, h, :], w3[:, k:k + 1],
                                            h2T[:, k, HALF * h:HALF * h + HALF], start=(k == 0), stop=(k == O2 - 1),
                                            skip_group_check=True)
            last.then_inc(y_summed, 1)

        @block.vector
        def _(dve):
            nc.vector.memset(pick[:, :], 0.0).then_inc(pick_zeroed, 1)
            nc.vector.memset(wsplit[:, 1, 0:DIM].bitcast(FP32), 0.0).then_inc(pads_zeroed, 1)
            dve.wait_ge(pick_zeroed, 1)
            nc.vector.memset(pick[0:DIM, 30:31], 1.0).then_inc(pick_made, 1)
            nc.vector.memset(pick[DIM:PART, 31:32], 1.0).then_inc(pick_made, 1)

            def weights_low(n, c):
                dve.wait_ge(w_high, n)
                cols = weights_chunk(n, c)
                nc.vector.tensor_tensor(wsplit[DIM:PART, n % 2, cols], wraw[DIM:PART, n % RAWRING, cols],
                                        wsplit[DIM:PART, n % 2, cols].bitcast(FP32), ALU.subtract).then_inc(w_low, 1)

            def table_low_part(n):
                dve.wait_ge(table_high, n + 1)
                nc.vector.tensor_tensor(table_split[0:TABLE_PART, n, :, 1, :], table_raw[0:TABLE_PART, n],
                                        table_split[0:TABLE_PART, n, :, 0, :].bitcast(FP32), ALU.subtract).then_inc(table_low, 1)

            def onehots(n):
                dve.wait_ge(ids_wide_ready, n + 1)
                for k in range(TABLE_PARTS):
                    o = n * TABLE_PARTS + k
                    if o >= ONEHOTS:
                        dve.wait_ge(onehot_used, o - ONEHOTS + 1)
                    nc.vector.tensor_scalar(onehot[0:TABLE_PART, o % ONEHOTS, :], ids_wide[0:TABLE_PART, n, :],
                                            table_row_f[0:TABLE_PART, k:k + 1], None, ALU.is_equal).then_inc(onehot_ready, 1)

            def looked_up(n):
                dve.wait_ge(x_high, n + 1)
                at = side(n)
                nc.vector.tensor_tensor(xT[at, (FIELDS - 1 - n) // 2, :], xsplit[at, n % XRING, 0, :].bitcast(FP32),
                                        xsplit[at, n % XRING, 1, :].bitcast(FP32), ALU.add).then_inc(x_low, 1)

            def field_low(n):
                if n < LOOKED:
                    looked_up(n)
                    return
                dve.wait_ge(x_high, n + 1)
                dve.wait_ge(x_ready, n - LOOKED + 1)
                u = FIELD_USE[n]
                nc.vector.tensor_tensor(xsplit[:, n % XRING, 1, :], ring[:, u % LRING, :, :].rearrange("p h c -> p (h c)"),
                                        xsplit[:, n % XRING, 0, :].bitcast(FP32), ALU.subtract).then_inc(x_low, 1)

            dve.wait_ge(ids_in, 16)
            nc.vector.tensor_copy(ids_f[:, :, :], ids_sb[:, :, FIELDS - LOOKED:FIELDS])
            dve.wait_ge(rows_numbered, 1)
            nc.vector.tensor_copy(table_row_f[:, :], table_row[:, :]).then_inc(numbers_ready, 1)
            dve.wait_ge(numbers_ready, 1)
            for n in range(AT_ONCE + 1):
                if n < LOOKED:
                    table_low_part(n)
                    onehots(n)
                if n == 0:
                    weights_low(1, 0)
                else:
                    field_low(n - 1)
            for n, turn in enumerate(TURNS):
                for k, (i, m) in enumerate(turn):
                    b = FIRST[n] + k
                    u = BLOCK_USE[b]
                    dve.wait_ge(left_ready, b + 1)
                    if k == 0:
                        field_ready(dve, n - 1)
                    if is_half(b):
                        e = HALF_BLOCKS.index(b)
                        if e % 2 == 0 and e // 2 >= HALF_RING:
                            dve.wait_ge(groups_summed, SLAB[HALF_BLOCKS[e - 2 * HALF_RING]] // GROUP + 1)
                        top, to = slice(DIM, PART), slice(DIM * (e % 2), DIM * (e % 2) + DIM)
                    else:
                        if FULL.index(b) >= PRING:
                            dve.wait_ge(groups_summed, SLAB[FULL[FULL.index(b) - PRING]] // GROUP + 1)
                        top = to = slice(0, PART)
                    nc.vector.tensor_tensor(slab(b)[to, :], ring[top, u % LRING, :, :].rearrange("p h c -> p (h c)"),
                                            xT[top, m, :], ALU.mult).then_inc(prod_ready, 1)
                    if k == 0 and n + 1 < FIELDS and FIELD_IN[n + 1] is not None and AT_ONCE < FIELD_IN[n + 1] < LOOKED:
                        table_low_part(FIELD_IN[n + 1])
                        onehots(FIELD_IN[n + 1])
                    if n + 1 < POOL_FROM:
                        for c in range(chunks(n + 1)):
                            if k == min(CHUNK * c, len(turn) - 1):
                                weights_low(n + 1, c)
                    if k == PREPARED_AFTER[n]:
                        field_low(FIELD_IN[n])

            dve.wait_ge(y_summed, 1)
            nc.vector.tensor_copy(y_columns(1), ring[32:33, (O1 + O2) % LRING, 1, :].rearrange("o (t p) -> o t p", p=PART)).then_inc(y_ready, 1)

        @block.scalar
        def _(act):
            def copy_rows(n):
                g = n - LOOKED
                act.wait_ge(rows_in[g % ROWRING], 16 * TILES * (g // ROWRING + 1))
                nc.scalar.copy(rows[:, g % ROWRING, :, 1, :], rows[:, g % ROWRING, :, 0, :]).then_inc(rows_twice, 1)

            def copy_field(n):
                u = FIELD_USE[n]
                if n < LOOKED:
                    act.wait_ge(onehot_used, TABLE_PARTS * (n + 1))
                else:
                    act.wait_ge(x_transposed, n - LOOKED + 1)
                if n > XRING:
                    act.wait_ge(left_ready, FIRST[n - XRING + 1])
                flat = ring[:, u % LRING, :, :].rearrange("p h c -> p (h c)")
                if n < LOOKED:
                    if n >= XRING:
                        act.wait_ge(x_low, n - XRING + 1)
                    for part in range(2):
                        for to in (0, DIM):
                            last = nc.scalar.copy(xsplit[to:to + DIM, n % XRING, part, :], flat[DIM * part:DIM * part + DIM, :])
                    last.then_inc(x_high, 1)
                else:
                    nc.scalar.copy(xsplit[:, n % XRING, 0, :], flat).then_inc(x_high, 1)
                    nc.scalar.copy(xT[side(n), (FIELDS - 1 - n) // 2, :], flat[side(n), :]).then_inc(x_ready, 1)

            def weights_high(n):
                i = FIELDS - 1 - n
                act.wait_ge(w_in[n % RAWRING], 32 * ((n - 1) // RAWRING + 1))
                if n > 2:
                    act.wait_ge(left_ready, FIRST[n - 1])
                cols = slice(DIM * (1 - i % 2), PART * len(TURNS[n]))
                nc.scalar.copy(wsplit[:, n % 2, cols], wraw[:, n % RAWRING, cols]).then_inc(w_high, 1)

            def copy_part(g):
                part = g // GROUPS_PER_KT
                act.wait_ge(groups_summed, g + 1)
                nc.scalar.copy(zT[:, part, :], zacc[:, :, :].rearrange("p h c -> p (h c)")).then_inc(z_ready, 1)

            for n in range(LOOKED):
                act.wait_ge(ids_spread, n + 1)
                nc.scalar.copy(ids_wide[:, n, :], ring[:, n % LRING, :, :].rearrange("p h c -> p (h c)")).then_inc(ids_wide_ready, 1)
                act.wait_ge(tables_in[n], 16)
                nc.scalar.copy(table_split[0:TABLE_PART, n, :, 0, :], table_raw[0:TABLE_PART, n]).then_inc(table_high, 1)
            weights_high(1)
            for n in range(AT_ONCE):
                copy_field(n)
                if n == EARLY:
                    for m in range(LOOKED, AT_ONCE):
                        copy_rows(m)
            for n, turn in enumerate(TURNS):
                if turn and n + 1 < FIELDS:
                    weights_high(n + 1)
                if n >= 1 and n + 1 < FIELDS and FIELD_IN[n + 1] is not None and FIELD_IN[n + 1] >= LOOKED:
                    copy_rows(FIELD_IN[n + 1])
                for k in range(len(turn)):
                    if k == PREPARED_AFTER[n]:
                        copy_field(FIELD_IN[n])
                    g = group_after(FIRST[n] + k)
                    if g is not None and closes_part(g):
                        copy_part(g)
            copy_part(GROUPS - 1)

            act.wait_ge(consts_in, 16 * 4)
            for o in range(O1):
                act.wait_ge(h1_summed, o + 1)
                nc.scalar.activation(h1T[:, o, :], ring[:, o % LRING, :, :].rearrange("p h c -> p (h c)"), ACT.Relu,
                                     bias=b1[:, o:o + 1]).then_inc(h1_ready, 1)
            for o in range(O2):
                act.wait_ge(h2_summed, o + 1)
                nc.scalar.activation(h2T[:, o, :], ring[:, (O1 + o) % LRING, :, :].rearrange("p h c -> p (h c)"), ACT.Relu,
                                     bias=b2[:, o:o + 1]).then_inc(h2_ready, 1)
            act.wait_ge(y_summed, 1)
            nc.scalar.copy(y_columns(0), ring[0:1, (O1 + O2) % LRING, 0, :].rearrange("o (t p) -> o t p", p=PART)).then_inc(y_ready, 1)


TABLES = [f"tbl_{f}" for f in range(FIELDS)]
INPUTS = ["dense_ctx", "ids", *TABLES, "W_top1", "b_top1", "W_top2", "b_top2", "W_top3", "L0_rec_W"]


def kernel(**inputs):
    import numpy as np
    import concourse.bacc as bacc
    from concourse.bass_utils import run_bass_kernel_spmd

    nc = bacc.Bacc("TRN2", target_bir_lowering=False, num_devices=1)
    arrays, aps = {}, {}
    for name in INPUTS:
        a = np.ascontiguousarray(inputs[name])
        arrays[f"in_{name}"] = a
        aps[name] = nc.dram_tensor(f"in_{name}", a.shape, mybir.dt.from_np(a.dtype), kind="ExternalInput").ap()
    y = nc.dram_tensor("out_y", (BATCH, 1), FP32, kind="ExternalOutput").ap()
    build(nc, aps["dense_ctx"], aps["ids"], [aps[t] for t in TABLES], aps["W_top1"], aps["b_top1"],
          aps["W_top2"], aps["b_top2"], aps["W_top3"], aps["L0_rec_W"], y)
    r = run_bass_kernel_spmd(nc, [arrays], core_ids=[0])
    return r.results[0]["out_y"]
```
